# Optimizing a Trainium2 kernel written in Bass

```python
import numpy as np
import jax
import jax.numpy as jnp

def _softmax(x, axis=-1):
    return jax.nn.softmax(x, axis=axis)

def _gelu(x):
    return jax.nn.gelu(x, approximate=True)

def _silu(x):
    return jax.nn.silu(x)

def _sigmoid(x):
    return jax.nn.sigmoid(x)

def _layernorm(x, axis=-1, eps=1e-05):
    m = jnp.mean(x, axis=axis, keepdims=True)
    v = jnp.var(x, axis=axis, keepdims=True)
    return (x - m) / jnp.sqrt(v + eps)

def _scatter_add(tgt, idx, src, axis=0):
    return tgt.at[idx].add(src)

def _segment_sum(src, seg, n):
    return jax.ops.segment_sum(src, seg, n)
kernel_name = 'mk_xattn_seq_d2_seqx_r8_88ffeb'

def setup_inputs(seed: int=0):
    np.random.seed(seed)
    _w = jnp.asarray

    def _rec_inputs():
        import jax
        import jax.numpy as jnp
        _rk = jax.random.key(seed)
        x = -0.0002928 + 1 * jax.random.normal(jax.random.fold_in(_rk, 1), (32, 64, 128), jnp.float32)
        _lenS = 64 - jax.random.randint(jax.random.fold_in(_rk, 7), (32,), 0, max(1, 64 // 4) + 1, jnp.int32)
        _lenS2 = 64 - jax.random.randint(jax.random.fold_in(_rk, 8), (32,), 0, max(1, 64 // 4) + 1, jnp.int32)
        _ctx_1024P = jax.random.normal(jax.random.fold_in(_rk, 11), (32, 16, 128), jnp.float32)
        _ctx_1024c = jax.random.dirichlet(jax.random.fold_in(_rk, 511), 0.3 * jnp.ones((16,), jnp.float32), (32, 64))
        _ctx_1024t = jnp.einsum('bsk,bkd->bsd', _ctx_1024c, _ctx_1024P)
        _ctx_1024t = _ctx_1024t * jax.lax.rsqrt(jnp.mean(jnp.square(_ctx_1024t)) + 1e-12) * 0.953939
        ctx_1024 = -1.39393e-06 + 0.999914 * (_ctx_1024t + 0.3 * jax.random.normal(jax.random.fold_in(_rk, 611), (32, 64, 128), jnp.float32))
        _validS = jnp.arange(64)[None, :] < _lenS[:, None]
        _validS2 = jnp.arange(64)[None, :] < _lenS2[:, None]
        _causal = jnp.tril(jnp.ones((64, 64), dtype=bool))
        mask_BxS2_bf1 = jnp.ones((32, 64), dtype=bool)
        return (x, ctx_1024, mask_BxS2_bf1)
    x, ctx_1024, mask_BxS2_bf1 = _rec_inputs()

    def _L0_xattn_setup():
        import jax, jax.numpy as jnp
        import numpy as np
        import math
        E = 128
        H = 16
        DK = 64
        DV = 64
        B = 2
        S = 256
        NEG_INF = float('-inf')

        def _layer_norm(x, gamma, beta, eps=1e-12):
            mean = x.mean(-1, keepdims=True)
            var = ((x - mean) ** 2).mean(-1, keepdims=True)
            return gamma * (x - mean) / jnp.sqrt(var + eps) + beta

        def _mha(q_in, k_in, v_in, wq, bq, wk, bk, wv, bv, wo, bo, padding_mask, causal):
            Bq, Sq, _ = q_in.shape
            Sk = k_in.shape[1]
            q = (q_in @ wq + bq).reshape(Bq, Sq, H, DK).transpose(0, 2, 1, 3)
            k = (k_in @ wk + bk).reshape(Bq, Sk, H, DK).transpose(0, 2, 1, 3)
            v = (v_in @ wv + bv).reshape(Bq, Sk, H, DV).transpose(0, 2, 1, 3)
            scores = jnp.einsum('bhqd,bhkd->bhqk', q, k)
            if causal:
                causal_mask = jnp.triu(jnp.ones((Sq, Sk), dtype=bool), k=1)
                scores = jnp.where(causal_mask[None, None], NEG_INF, scores)
            if padding_mask is not None:
                scores = jnp.where(padding_mask[:, None, None, :], scores, NEG_INF)
            attn = jax.nn.softmax(scores / math.sqrt(DK), axis=-1)
            attn = jnp.nan_to_num(attn, nan=0.0, posinf=0.0, neginf=0.0)
            out = jnp.einsum('bhqk,bhkd->bhqd', attn, v)
            out = out.transpose(0, 2, 1, 3).reshape(Bq, Sq, H * DV)
            return out @ wo + bo
        key = jax.random.key(seed)
        ks = jax.random.split(key, 24)
        s = 0.02

        def w(i, shape):
            return (s * jax.random.normal(ks[i], shape)).astype(jnp.float32)
        inp = {'input': jax.random.normal(ks[0], (B, S, E), dtype=jnp.float32), 'encoder_output': jax.random.normal(ks[1], (B, S, E), dtype=jnp.float32), 'src_mask': jnp.ones((B, S), dtype=bool), 'trg_mask': jnp.ones((B, S), dtype=bool), 'sa_wq': w(2, (E, H * DK)), 'sa_bq': jnp.zeros((H * DK,), jnp.float32), 'sa_wk': w(3, (E, H * DK)), 'sa_bk': jnp.zeros((H * DK,), jnp.float32), 'sa_wv': w(4, (E, H * DV)), 'sa_bv': jnp.zeros((H * DV,), jnp.float32), 'sa_wo': w(5, (H * DV, E)), 'sa_bo': jnp.zeros((E,), jnp.float32), 'ca_wq': w(6, (E, H * DK)), 'ca_bq': jnp.zeros((H * DK,), jnp.float32), 'ca_wk': w(7, (E, H * DK)), 'ca_bk': jnp.zeros((H * DK,), jnp.float32), 'ca_wv': w(8, (E, H * DV)), 'ca_bv': jnp.zeros((H * DV,), jnp.float32), 'ca_wo': w(9, (H * DV, E)), 'ca_bo': jnp.zeros((E,), jnp.float32), 'ffn_w1': w(10, (E, 4 * E)), 'ffn_b1': jnp.zeros((4 * E,), jnp.float32), 'ffn_w2': w(11, (4 * E, E)), 'ffn_b2': jnp.zeros((E,), jnp.float32), 'ln1_g': jnp.ones((E,), jnp.float32), 'ln1_b': jnp.zeros((E,), jnp.float32), 'ln2_g': jnp.ones((E,), jnp.float32), 'ln2_b': jnp.zeros((E,), jnp.float32), 'ln3_g': jnp.ones((E,), jnp.float32), 'ln3_b': jnp.zeros((E,), jnp.float32)}
        return inp
    _L0_xattn_all = _L0_xattn_setup()
    _L0_xattn_in = {k: v for k, v in _L0_xattn_all.items() if k in ('sa_wq', 'sa_bq', 'sa_wk', 'sa_bk', 'sa_wv', 'sa_bv', 'sa_wo', 'sa_bo', 'ca_wq', 'ca_bq', 'ca_wk', 'ca_bk', 'ca_wv', 'ca_bv', 'ca_wo', 'ca_bo', 'ffn_w1', 'ffn_b1', 'ffn_w2', 'ffn_b2', 'ln1_g', 'ln1_b', 'ln2_g', 'ln2_b', 'ln3_g', 'ln3_b')}
    del _L0_xattn_all

    def _L1_xattn_setup():
        import jax, jax.numpy as jnp
        import numpy as np
        NUM_HEADS = 16
        HEAD_DIM = 64
        D_MODEL = 128
        ROPE_BASE = 10000.0

        def rope(x):
            B, S, H, D = x.shape
            inv_freq = 1.0 / ROPE_BASE ** (jnp.arange(0, D, 2, dtype=jnp.float32) / D)
            t = jnp.arange(S, dtype=jnp.float32)
            freqs = jnp.einsum('s,d->sd', t, inv_freq)
            cos = jnp.cos(freqs)[None, :, None, :]
            sin = jnp.sin(freqs)[None, :, None, :]
            x1, x2 = (x[..., 0::2], x[..., 1::2])
            r1 = x1 * cos - x2 * sin
            r2 = x2 * cos + x1 * sin
            out = jnp.stack([r1, r2], axis=-1).reshape(B, S, H, D)
            return out.astype(x.dtype)
        key = jax.random.key(seed)
        ks = jax.random.split(key, 8)
        B, Sq, Skv = (4, 128, 256)
        d = D_MODEL
        hd = NUM_HEADS * HEAD_DIM
        scale = 1.0 / np.sqrt(d)
        return {'decoder_query': jax.random.normal(ks[0], (B, Sq, d), jnp.float32), 'encoder_key_value': jax.random.normal(ks[1], (B, Skv, d), jnp.float32), 'mask': jnp.ones((B, Skv), dtype=bool), 'Wq': jax.random.normal(ks[2], (d, hd), jnp.float32) * scale, 'Wk': jax.random.normal(ks[3], (d, hd), jnp.float32) * scale, 'Wv': jax.random.normal(ks[4], (d, hd), jnp.float32) * scale, 'Wo': jax.random.normal(ks[5], (hd, d), jnp.float32) * (1.0 / np.sqrt(hd)), 'ln_gamma': jnp.ones((d,), jnp.float32), 'ln_beta': jnp.zeros((d,), jnp.float32)}
    _L1_xattn_all = _L1_xattn_setup()
    _L1_xattn_in = {k: v for k, v in _L1_xattn_all.items() if k in ('Wq', 'Wk', 'Wv', 'Wo', 'ln_gamma', 'ln_beta')}
    del _L1_xattn_all
    return {'x': x, 'ctx_1024': ctx_1024, 'mask_BxS2_bf1': mask_BxS2_bf1, 'L0_xattn_sa_wq': _L0_xattn_in['sa_wq'], 'L0_xattn_sa_bq': _L0_xattn_in['sa_bq'], 'L0_xattn_sa_wk': _L0_xattn_in['sa_wk'], 'L0_xattn_sa_bk': _L0_xattn_in['sa_bk'], 'L0_xattn_sa_wv': _L0_xattn_in['sa_wv'], 'L0_xattn_sa_bv': _L0_xattn_in['sa_bv'], 'L0_xattn_sa_wo': _L0_xattn_in['sa_wo'], 'L0_xattn_sa_bo': _L0_xattn_in['sa_bo'], 'L0_xattn_ca_wq': _L0_xattn_in['ca_wq'], 'L0_xattn_ca_bq': _L0_xattn_in['ca_bq'], 'L0_xattn_ca_wk': _L0_xattn_in['ca_wk'], 'L0_xattn_ca_bk': _L0_xattn_in['ca_bk'], 'L0_xattn_ca_wv': _L0_xattn_in['ca_wv'], 'L0_xattn_ca_bv': _L0_xattn_in['ca_bv'], 'L0_xattn_ca_wo': _L0_xattn_in['ca_wo'], 'L0_xattn_ca_bo': _L0_xattn_in['ca_bo'], 'L0_xattn_ffn_w1': _L0_xattn_in['ffn_w1'], 'L0_xattn_ffn_b1': _L0_xattn_in['ffn_b1'], 'L0_xattn_ffn_w2': _L0_xattn_in['ffn_w2'], 'L0_xattn_ffn_b2': _L0_xattn_in['ffn_b2'], 'L0_xattn_ln1_g': _L0_xattn_in['ln1_g'], 'L0_xattn_ln1_b': _L0_xattn_in['ln1_b'], 'L0_xattn_ln2_g': _L0_xattn_in['ln2_g'], 'L0_xattn_ln2_b': _L0_xattn_in['ln2_b'], 'L0_xattn_ln3_g': _L0_xattn_in['ln3_g'], 'L0_xattn_ln3_b': _L0_xattn_in['ln3_b'], 'L1_xattn_Wq': _L1_xattn_in['Wq'], 'L1_xattn_Wk': _L1_xattn_in['Wk'], 'L1_xattn_Wv': _L1_xattn_in['Wv'], 'L1_xattn_Wo': _L1_xattn_in['Wo'], 'L1_xattn_ln_gamma': _L1_xattn_in['ln_gamma'], 'L1_xattn_ln_beta': _L1_xattn_in['ln_beta']}

def reference(x, ctx_1024, mask_BxS2_bf1, L0_xattn_sa_wq, L0_xattn_sa_bq, L0_xattn_sa_wk, L0_xattn_sa_bk, L0_xattn_sa_wv, L0_xattn_sa_bv, L0_xattn_sa_wo, L0_xattn_sa_bo, L0_xattn_ca_wq, L0_xattn_ca_bq, L0_xattn_ca_wk, L0_xattn_ca_bk, L0_xattn_ca_wv, L0_xattn_ca_bv, L0_xattn_ca_wo, L0_xattn_ca_bo, L0_xattn_ffn_w1, L0_xattn_ffn_b1, L0_xattn_ffn_w2, L0_xattn_ffn_b2, L0_xattn_ln1_g, L0_xattn_ln1_b, L0_xattn_ln2_g, L0_xattn_ln2_b, L0_xattn_ln3_g, L0_xattn_ln3_b, L1_xattn_Wq, L1_xattn_Wk, L1_xattn_Wv, L1_xattn_Wo, L1_xattn_ln_gamma, L1_xattn_ln_beta):
    import jax
    import jax.numpy as jnp

    def _L0_xattn_ref(input, encoder_output, src_mask, trg_mask, sa_wq, sa_bq, sa_wk, sa_bk, sa_wv, sa_bv, sa_wo, sa_bo, ca_wq, ca_bq, ca_wk, ca_bk, ca_wv, ca_bv, ca_wo, ca_bo, ffn_w1, ffn_b1, ffn_w2, ffn_b2, ln1_g, ln1_b, ln2_g, ln2_b, ln3_g, ln3_b):
        import jax, jax.numpy as jnp
        import numpy as np
        import math
        E = 128
        H = 16
        DK = 64
        DV = 64
        B = 2
        S = 256
        NEG_INF = float('-inf')

        def _layer_norm(x, gamma, beta, eps=1e-12):
            mean = x.mean(-1, keepdims=True)
            var = ((x - mean) ** 2).mean(-1, keepdims=True)
            return gamma * (x - mean) / jnp.sqrt(var + eps) + beta

        def _mha(q_in, k_in, v_in, wq, bq, wk, bk, wv, bv, wo, bo, padding_mask, causal):
            Bq, Sq, _ = q_in.shape
            Sk = k_in.shape[1]
            q = (q_in @ wq + bq).reshape(Bq, Sq, H, DK).transpose(0, 2, 1, 3)
            k = (k_in @ wk + bk).reshape(Bq, Sk, H, DK).transpose(0, 2, 1, 3)
            v = (v_in @ wv + bv).reshape(Bq, Sk, H, DV).transpose(0, 2, 1, 3)
            scores = jnp.einsum('bhqd,bhkd->bhqk', q, k)
            if causal:
                causal_mask = jnp.triu(jnp.ones((Sq, Sk), dtype=bool), k=1)
                scores = jnp.where(causal_mask[None, None], NEG_INF, scores)
            if padding_mask is not None:
                scores = jnp.where(padding_mask[:, None, None, :], scores, NEG_INF)
            attn = jax.nn.softmax(scores / math.sqrt(DK), axis=-1)
            attn = jnp.nan_to_num(attn, nan=0.0, posinf=0.0, neginf=0.0)
            out = jnp.einsum('bhqk,bhkd->bhqd', attn, v)
            out = out.transpose(0, 2, 1, 3).reshape(Bq, Sq, H * DV)
            return out @ wo + bo
        residual = input
        sa = _mha(input, input, input, sa_wq, sa_bq, sa_wk, sa_bk, sa_wv, sa_bv, sa_wo, sa_bo, trg_mask, causal=True)
        x = _layer_norm(sa + residual, ln1_g, ln1_b)
        residual = x
        ca = _mha(x, encoder_output, encoder_output, ca_wq, ca_bq, ca_wk, ca_bk, ca_wv, ca_bv, ca_wo, ca_bo, src_mask, causal=False)
        x = _layer_norm(ca + residual, ln2_g, ln2_b)
        residual = x
        h = jax.nn.relu(x @ ffn_w1 + ffn_b1)
        x = _layer_norm(h @ ffn_w2 + ffn_b2 + residual, ln3_g, ln3_b)
        return x

    def _L1_xattn_ref(decoder_query, encoder_key_value, mask, Wq, Wk, Wv, Wo, ln_gamma, ln_beta):
        import jax, jax.numpy as jnp
        import numpy as np
        NUM_HEADS = 16
        HEAD_DIM = 64
        D_MODEL = 128
        ROPE_BASE = 10000.0

        def rope(x):
            B, S, H, D = x.shape
            inv_freq = 1.0 / ROPE_BASE ** (jnp.arange(0, D, 2, dtype=jnp.float32) / D)
            t = jnp.arange(S, dtype=jnp.float32)
            freqs = jnp.einsum('s,d->sd', t, inv_freq)
            cos = jnp.cos(freqs)[None, :, None, :]
            sin = jnp.sin(freqs)[None, :, None, :]
            x1, x2 = (x[..., 0::2], x[..., 1::2])
            r1 = x1 * cos - x2 * sin
            r2 = x2 * cos + x1 * sin
            out = jnp.stack([r1, r2], axis=-1).reshape(B, S, H, D)
            return out.astype(x.dtype)
        B, Sq, d = decoder_query.shape
        Skv = encoder_key_value.shape[1]
        H, Dh = (NUM_HEADS, HEAD_DIM)
        q = (decoder_query @ Wq).reshape(B, Sq, H, Dh)
        k = (encoder_key_value @ Wk).reshape(B, Skv, H, Dh)
        v = (encoder_key_value @ Wv).reshape(B, Skv, H, Dh)
        q = rope(q)
        k = rope(k)
        q = q.transpose(0, 2, 1, 3) * (1.0 / jnp.sqrt(jnp.asarray(Dh, q.dtype)))
        k = k.transpose(0, 2, 1, 3)
        v = v.transpose(0, 2, 1, 3)
        scores = jnp.einsum('bhqd,bhkd->bhqk', q, k)
        m = mask[:, None, None, :]
        scores = jnp.where(m, scores, jnp.asarray(-1000000000.0, scores.dtype))
        attn = jax.nn.softmax(scores, axis=-1)
        out = jnp.einsum('bhqk,bhkd->bqhd', attn, v).reshape(B, Sq, H * Dh)
        out = out @ Wo
        x = decoder_query + out
        mu = jnp.mean(x, axis=-1, keepdims=True)
        var = jnp.var(x, axis=-1, keepdims=True)
        y = (x - mu) * jax.lax.rsqrt(var + 0.001) * ln_gamma + ln_beta
        return y
    x = _L0_xattn_ref(x, ctx_1024, mask_BxS2_bf1, mask_BxS2_bf1, L0_xattn_sa_wq, L0_xattn_sa_bq, L0_xattn_sa_wk, L0_xattn_sa_bk, L0_xattn_sa_wv, L0_xattn_sa_bv, L0_xattn_sa_wo, L0_xattn_sa_bo, L0_xattn_ca_wq, L0_xattn_ca_bq, L0_xattn_ca_wk, L0_xattn_ca_bk, L0_xattn_ca_wv, L0_xattn_ca_bv, L0_xattn_ca_wo, L0_xattn_ca_bo, L0_xattn_ffn_w1, L0_xattn_ffn_b1, L0_xattn_ffn_w2, L0_xattn_ffn_b2, L0_xattn_ln1_g, L0_xattn_ln1_b, L0_xattn_ln2_g, L0_xattn_ln2_b, L0_xattn_ln3_g, L0_xattn_ln3_b)
    x = _L1_xattn_ref(x, ctx_1024, mask_BxS2_bf1, L1_xattn_Wq, L1_xattn_Wk, L1_xattn_Wv, L1_xattn_Wo, L1_xattn_ln_gamma, L1_xattn_ln_beta)
    return x

_drawn_inputs = setup_inputs


def setup_inputs(seed=0):
    import zlib

    import numpy as np

    out = dict(_drawn_inputs(seed))
    spreads = {'L0_xattn_sa_bq': (0.0, 0.8),
     'L0_xattn_sa_bk': (0.0, 0.8),
     'L0_xattn_sa_bv': (0.0, 0.1),
     'L0_xattn_sa_bo': (0.0, 0.1),
     'L0_xattn_ca_bq': (0.0, 0.8),
     'L0_xattn_ca_bk': (0.0, 0.8),
     'L0_xattn_ca_bv': (0.0, 0.1),
     'L0_xattn_ca_bo': (0.0, 0.1),
     'L0_xattn_ffn_b1': (0.0, 0.27),
     'L0_xattn_ffn_b2': (0.0, 0.1),
     'L0_xattn_ln1_g': (1.0, 0.2),
     'L0_xattn_ln1_b': (0.0, 0.1),
     'L0_xattn_ln2_g': (1.0, 0.2),
     'L0_xattn_ln2_b': (0.0, 0.1),
     'L0_xattn_ln3_g': (1.0, 0.2),
     'L0_xattn_ln3_b': (0.0, 0.1),
     'L1_xattn_ln_gamma': (1.0, 0.2),
     'L1_xattn_ln_beta': (0.0, 0.1)}
    factors = {'L0_xattn_sa_wq': 8.0, 'L0_xattn_sa_wk': 8.0, 'L0_xattn_ca_wq': 8.0, 'L0_xattn_ca_wk': 8.0}
    for name, (base, spread) in spreads.items():
        noise = np.random.default_rng([zlib.crc32(name.encode()), seed]).standard_normal(out[name].shape)
        drawn = base * np.exp(spread * noise) if base else spread * noise
        out[name] = jnp.asarray(drawn.astype(out[name].dtype))
    for name, factor in factors.items():
        out[name] = (out[name] * factor).astype(out[name].dtype)
    return out
```

```python
from contextlib import ExitStack

import numpy as np
import concourse.bass as bass
from concourse import mybir

ALU = mybir.AluOpType
ACT = mybir.ActivationFunctionType
F32 = mybir.dt.float32
F32R = mybir.dt.float32r
BF16 = mybir.dt.bfloat16
AX_X = mybir.AxisListType.X

B, S, E = 32, 64, 128
H, D = 16, 64
PAIRS = H // 2
UNITS = B // 2
CU = 2
CT = CU * 128
LAYERS = 3
N = LAYERS * UNITS
FFN = 512
FC = FFN // 128
HALF = PAIRS // 2
NEG = -1.0e30
PERIOD = 4



def projected(u):
    g = u // 2 + 1
    return g if g < N // 2 else None


def ffn_chunk(u):
    g = (u - 3) // 2
    return g if u % 2 and UNITS // 2 <= g < UNITS else None


def attends(u):
    return 0 <= u < N


def finishes(u):
    return 0 <= u - 1 < N


def fills(u):
    out = []
    rotary = projected(u) is not None and projected(u) * 2 // UNITS == 2
    if u % 2 == 0 and projected(u) is not None:
        out.append(("T", 0, "AD"))
    items = []
    values = [("V", j, "A") for j in range(2)] if attends(u) else []
    if projected(u) is not None:
        name = "K" if u % 2 else "Q"
        for j in range(4):
            if rotary:
                items += [(name + "a", j, "D"), (name + "b", j, "D")]
            else:
                items.append((name, j, "AD" if u % 2 else "AD"[j % 2]))
    if u > 0 and u % UNITS == 0:
        items = items + values
    elif rotary and u >= 2 * UNITS:
        items = values[:1] + items + values[1:] if u % 2 == 0 else \
            items[:2] + values[:1] + items[2:4] + values[1:] + items[4:]
    else:
        items = values + items
    if ffn_chunk(u) is not None:
        items = items[:3] + [("FT", 0, "AD"), items[3], ("F1", 0, "A"), items[4], ("F1", 1, "D")] + items[5:]
        items.append(("F2", 0, "D"))
    return out + items


def plan(u):
    anchors = [("S", j) for j in range(2)] if attends(u) else []
    if finishes(u):
        anchors += [("AV", 0), ("AV", 1), ("OT", 0), ("OT", 1)]
    if attends(u):
        anchors += [("PT", 0), ("PT", 1)]
    if finishes(u):
        anchors.append(("Y", 0))
    todo = [(name, j, at) for at, (name, j, _) in enumerate(fills(u))]
    gaps = max(len(anchors) - 2, 1)
    if u % 2 and u >= 2 * UNITS and ffn_chunk(u) is None and gaps > 2:
        gaps -= 2
    out = []
    for k, anchor in enumerate(anchors):
        out.append(anchor)
        out += [f for f in todo if f[2] * gaps // len(todo) == k]
    return out if anchors else todo


class Tally:

    def __init__(self, events):
        self.events = {u: [tuple(e) for e in events(u)] for u in range(-2, N + 2)}

    def before(self, u):
        return sum(len(self.events[v]) for v in range(-2, u))

    def at(self, u, *event):
        return self.before(u) + self.events[u].index(event) + 1

    def after(self, u):
        return self.before(u + 1)


def attn(*names):
    return lambda u: [(n,) for n in names] if attends(u) else []


FILL = Tally(lambda u: [(n, j) for n, j, _ in fills(u)])
EMPTY_A = Tally(lambda u: [(n, j) for n, j, who in fills(u) if "A" in who])
EMPTY_D = Tally(lambda u: [(n, j) for n, j, who in fills(u) if "D" in who])
ALL_FILLS = [(u, n, j, who) for u in range(-2, N + 2) for n, j, who in fills(u)]
TURN = Tally(lambda u: ([("o", 0), ("o", 1)] if finishes(u) else []) + ([("p", 0), ("p", 1)] if attends(u) else []))
VSTEP = Tally(lambda u: ([("max", 0), ("max", 1)] if attends(u) else [])
              + ([("sum",), ("recip",)] if attends(u) else [])
              + ([("fstat", 0), ("fstat", 1), ("fmv", 0), ("fmv", 1)] if ffn_chunk(u) is not None else [])
              + ([("rinv",)] if attends(u) else [])
              + ([("stat",), ("mv",)] if finishes(u) else []))
LN_STEPS = ["eps", "rstd", "mr", "scaled", "norm", "gain"]
PSTEP = Tally(lambda u: ([("rbias",), ("rbo",), ("res",)] if finishes(u) else [])
              + ([("fres",)] if ffn_chunk(u) is not None else [])
              + ([("f" + n, v) for v in range(2) for n in LN_STEPS + ["out"]] if ffn_chunk(u) is not None else [])
              + ([(n, 0) for n in LN_STEPS + ["out"]] if finishes(u) else []))
ROTATED = Tally(lambda u: [(n, j) for n, j, _ in fills(u) if n == "Qb" or n == "Kb" and j < 3])
PARTS = Tally(lambda u: [(j,) for n, j, _ in fills(u) if n == "Kb" and j < 3])
LAST_ROTATED = Tally(lambda u: [(n, j) for n, j, _ in fills(u) if n == "Kb" and j == 3])
TWICE = Tally(attn(0, 1))
FIN2 = Tally(lambda u: [(0,), (1,)] if finishes(u) else [])
FIN1 = Tally(lambda u: [(0,)] if finishes(u) else [])


class Step:

    def __init__(self, u, i=None, times=1):
        self.u, self.i, self.times = u, i, times

    def value(self, count):
        v = [count(self.u + PERIOD * n) for n in range(self.times)]
        rise = v[1] - v[0] if self.times > 1 else 0
        assert all(b - a == rise for a, b in zip(v, v[1:])), (self.u, v)
        if self.times == 1 or rise == 0:
            return v[0]
        return self.i * rise + v[0]

    def wait(self, eng, sem, count, carrier=None):
        v = self.value(count)
        if not isinstance(v, int) or v > 0:
            eng.wait_ge(sem, v)
            if not isinstance(v, int) and carrier is not None:
                carrier()

    @property
    def layer(self):
        return self.u // UNITS


def stream(eng, step, before=None):
    for u in range(-2, 2):
        if before and u in before:
            before[u]()
        step(Step(u))
    for layer in range(LAYERS):
        first, times = layer * UNITS + 2, 3
        with eng.Fori(0, times) as i:
            for u in range(first, first + PERIOD):
                step(Step(u, i, times))
        for u in range(first + PERIOD * times, min((layer + 1) * UNITS + 2, N + 1)):
            step(Step(u))


def build(nc, a, out):
    ctx = ExitStack()
    with ctx:
        def sb(name, shape, dt=F32):
            return ctx.enter_context(nc.sbuf_tensor(name, shape, dt))

        def psum(name):
            return ctx.enter_context(nc.psum_tensor(name, [128, 512], F32))

        def sem(name):
            return ctx.enter_context(nc.semaphore(name))

        X = sb("X", [128, UNITS, E])
        C = sb("C", [128, UNITS, E])
        chunk_in = sb("chunk_in", [128, 2 * CU, E])
        inT_hi = sb("inT_hi", [128, 2, 2 * CT], F32R)
        inT_lo = sb("inT_lo", [128, 2, 2 * CT], F32R)
        w_raw = [sb(f"w{n}_raw", [128, H * D]) for n in "qkv"]
        w_hi = [sb(f"w{n}_hi", [128, H * D], F32R) for n in "qkv"]
        w_lo = [sb(f"w{n}_lo", [128, H * D], F32R) for n in "qkv"]
        sw_hi = [sb(f"sw{n}_hi", [128, H * D], F32R) for n in "qk"]
        sw_lo = [sb(f"sw{n}_lo", [128, H * D], F32R) for n in "qk"]
        wo = sb("wo", [128, 2, PAIRS, E])
        w1_hi = sb("w1_hi", [128, FFN], F32R)
        w1_lo = sb("w1_lo", [128, FFN], F32R)
        w2 = sb("w2", [128, FC, E])
        bq = sb("bq", [128, 2, PAIRS])
        bk = sb("bk", [128, 2, PAIRS])
        bv = sb("bv", [128, 2, PAIRS])
        b1 = sb("b1", [128, FC])
        bo = sb("bo", [128, 2, E])
        b2 = sb("b2", [128, E])
        gain = sb("gain", [128, 4, E])
        shift = sb("shift", [128, 4, E])
        bvwo = sb("bvwo", [128, 2, E])
        eye = sb("eye", [128, 128])
        eye_bf = sb("eye_bf", [128, 128], BF16)
        mask_u8 = sb("mask_u8", [128, UNITS, S], mybir.dt.uint8)
        mask = sb("mask", [128, 2, UNITS, S], BF16)
        valid = sb("valid", [128, LAYERS, UNITS])
        cos = sb("cos", [128, S])
        sin = sb("sin", [128, S])
        qT = sb("qT", [128, 2, PAIRS, CT])
        kT = sb("kT", [128, 2, PAIRS, 2 * CU, 128])
        vv = sb("vv", [128, 2, 2, PAIRS, 128])
        probs = sb("probs", [128, H, S])
        probsT = sb("probsT", [128, 2, 512])
        heads = sb("heads", [128, H, D])
        headsT = sb("headsT", [128, 2, 512])
        top = sb("top", [128, H])
        total = sb("total", [128, H])
        inv = sb("inv", [128, H])
        rinv = sb("rinv", [128, H])
        rope_a = sb("rope_a", [128, 2, 512])
        rope_b = sb("rope_b", [128, 2, 512])
        res = sb("res", [128, E])
        z = sb("z", [128, 2, E])
        zn = sb("zn", [128, E])
        stat = sb("stat", [128, 6])
        mv = sb("mv", [128, 2, 2])
        small = sb("small", [128, 3])
        minus_half = sb("minus_half", [128, 1])
        epsilon = sb("epsilon", [128, 2])
        carried = sb("carried", [128, 64], BF16)
        y_out = sb("y_out", [128, 2, E])
        x2 = sb("x2", [128, 4, E])
        x2T_hi = sb("x2T_hi", [128, CT], F32R)
        x2T_lo = sb("x2T_lo", [128, CT], F32R)
        hT = sb("hT", [128, FC, CT])
        w1_raw = hT[:, 0:2, :].rearrange("e c f -> e (c f)")
        fres = sb("fres", [128, 2, E])
        fz = sb("fz", [128, 2, E])
        fstat = sb("fstat", [128, 2, 6])
        fmv = sb("fmv", [128, 2, 2])

        ps_s = [psum(f"ps_s{j}") for j in range(2)]
        ps_t = [psum(f"ps_t{j}") for j in range(2)]
        ps_o = [psum(f"ps_o{j}") for j in range(2)]
        ps_p = [psum(f"ps_p{j}") for j in range(2)]

        x_loaded = sem("x_loaded")
        late_loaded = sem("late_loaded")
        const_loaded = sem("const_loaded")
        mask_loaded = sem("mask_loaded")
        w_loaded = [sem(f"w{n}_loaded") for n in "qkv"]
        wo_loaded = sem("wo_loaded")
        first_loaded = sem("first_loaded")
        w1_loaded = sem("w1_loaded")
        chunk_loaded = sem("chunk_loaded")
        w_hi_ready = [sem(f"w{n}_hi_ready") for n in "qkv"]
        swapped_ready = [sem(f"sw{n}_ready") for n in "qk"]
        w_ready = [sem(f"w{n}_ready") for n in "qkv"]
        setup_pool = sem("setup_pool")
        setup_dve = sem("setup_dve")
        bvwo_done = sem("bvwo_done")
        bvwo_read = sem("bvwo_read")
        filled = sem("filled")
        act_emptied = sem("act_emptied")
        dve_emptied = sem("dve_emptied")
        scored = sem("scored")
        shifted = sem("shifted")
        exped = sem("exped")
        turned = sem("turned")
        turn_read = sem("turn_read")
        weighted = sem("weighted")
        weighted_read = sem("weighted_read")
        outed = sem("outed")
        out_read = sem("out_read")
        dve_step = sem("dve_step")
        pool_step = sem("pool_step")
        rotated = sem("rotated")
        last_rotated = sem("last_rotated")
        rope_part = sem("rope_part")
        stored = [sem(f"stored{v}") for v in range(2)]

        block = ctx.enter_context(nc.Block())

        prefix = ["L0_xattn_sa_", "L0_xattn_ca_", "L1_xattn_"]

        def weight(layer, which):
            return a[prefix[layer] + (("w" if layer < 2 else "W") + which)]

        def rows(ap):
            return ap.partition_broadcast(128)

        def local(s, du):
            first = (s.u + du) % UNITS
            if s.times == 1:
                return first
            return s.i * PERIOD + first

        N_CONST = 14
        EYES, ZERO_K0, ZEROED, MASKED, W1_SPLIT = 4, 5, 9, 11, 13
        PADDED, STAGED, VALID = 2, 4, 7

        def new_weights(s, after_input=False):
            if s.u < 0:
                return {(-2, False): (0, 0), (-2, True): (0, 1), (-1, False): (0, 2)}.get((s.u, after_input))
            if s.times == 1 and not after_input:
                for n in range(3):
                    layer = (s.u + 2 - n) // UNITS
                    if (s.u + 2 - n) % UNITS == 0 and 0 < layer < LAYERS:
                        return layer, n
            return None

        def halves(t):
            return t[:, :].rearrange("e (i two) -> e i two", two=2)

        def add_keys(eng, s, j, h):
            rows_ = slice(64 * h, 64 * h + 64)
            dst = kT[rows_, projected(s.u) % 2, 2 * j:2 * j + 2, :, 64 * h:64 * h + 64]
            return eng.tensor_tensor(dst.rearrange("d p b t -> d (p b) t"),
                                     rope_a[rows_, j % 2, :].rearrange("d (b t) -> d b t", t=S),
                                     rope_b[rows_, j % 2, :].rearrange("d (b t) -> d b t", t=S), ALU.add)

        @block.sync
        def _(sp):
            tokens = a["x"].rearrange("(u b) s e -> (b s) u e", b=2)
            context = a["ctx_1024"].rearrange("(u b) s e -> (b s) u e", b=2)
            sp.dma_start(w_raw[0][:, :], weight(0, "q")).then_inc(w_loaded[0], 16)
            for part in range(2):
                sp.dma_start(chunk_in[:, CU * part:CU * part + CU, :], tokens[:, 0:CU, :]).then_inc(chunk_loaded, 16)
            sp.dma_start(w_raw[1][:, :], weight(0, "k")).then_inc(w_loaded[1], 16)
            for which, dst in (("q", bq), ("k", bk), ("v", bv)):
                for layer in range(2):
                    sp.dma_start(dst[:, layer, :], a[prefix[layer] + "b" + which]).then_inc(first_loaded, 16)
            for b in range(2):
                src = a["mask_BxS2_bf1"].rearrange("(u b) k -> b u k", b=2)[b]
                sp.dma_start(mask_u8[64 * b:64 * b + 64, :, :], src.partition_broadcast(64)).then_inc(mask_loaded, 16)
            sp.dma_start(w_raw[2][:, :], weight(0, "v")).then_inc(w_loaded[2], 16)
            sp.dma_start(X[:, :, :], tokens).then_inc(x_loaded, 16)
            for layer in range(2):
                sp.dma_start(bo[:, layer, :], rows(a[prefix[layer] + "bo"])).then_inc(const_loaded, 16)
                sp.dma_start(wo[:, layer, :, :], weight(layer, "o").rearrange("(p r) e -> r p e", r=128))\
                  .then_inc(wo_loaded, 16)
            sp.dma_start(cos[:, :], a["rope_cos"]).then_inc(const_loaded, 16)
            sp.dma_start(sin[:, :], a["rope_sin"]).then_inc(const_loaded, 16)
            for n, names in enumerate([("L0_xattn_ln1_g", "L0_xattn_ln1_b"), ("L0_xattn_ln2_g", "L0_xattn_ln2_b"),
                                       ("L0_xattn_ln3_g", "L0_xattn_ln3_b"), ("L1_xattn_ln_gamma", "L1_xattn_ln_beta")]):
                sp.dma_start(gain[:, n, :], rows(a[names[0]])).then_inc(const_loaded, 16)
                sp.dma_start(shift[:, n, :], rows(a[names[1]])).then_inc(const_loaded, 16)
            sp.dma_start(b1[:, :], a["L0_xattn_ffn_b1"]).then_inc(const_loaded, 16)
            sp.dma_start(b2[:, :], rows(a["L0_xattn_ffn_b2"])).then_inc(const_loaded, 16)
            sp.dma_start(w1_raw, a["L0_xattn_ffn_w1"]).then_inc(w1_loaded, 16)
            sp.dma_start(w2[:, :, :], a["L0_xattn_ffn_w2"].rearrange("(c r) e -> r c e", r=128)).then_inc(late_loaded, 16)
            sp.dma_start(C[:, :, :], context).then_inc(late_loaded, 16)
            result = out.rearrange("(u b) s e -> (b s) u e", b=2)

            def load_chunk(s):
                if s.u % 2 or s.u < 0 or projected(s.u) is None:
                    return
                layer = projected(s.u) * 2 // UNITS
                if s.u == UNITS - 2:
                    sp.wait_ge(late_loaded, 32)
                if s.u == 0:
                    sp.wait_ge(filled, FILL.at(-2, "T", 0))
                    sp.wait_ge(x_loaded, 16)
                else:
                    s.wait(sp, scored, lambda w: TWICE.at(w - 1, 0))
                src = bass.ds(local(s, 2), CU)
                sp.dma_start(chunk_in[:, 0:CU, :], X[:, src, :]).then_inc(chunk_loaded, 16)
                sp.dma_start(chunk_in[:, CU:2 * CU, :], (C if layer else X)[:, src, :]).then_inc(chunk_loaded, 16)

            def store(s):
                if s.u - 2 < 2 * UNITS:
                    return
                s.wait(sp, pool_step, lambda w: PSTEP.at(w - 1, "out", 0))
                v = s.u % 2
                sp.dma_start(result[:, bass.ds(local(s, -2), 1), :], y_out[:, v:v + 1, :]).then_inc(stored[v], 16)

            def step(s):
                load_chunk(s)
                if s.u in (1, UNITS + 1):
                    for n in range(3):
                        sp.wait_ge(w_ready[n], s.layer + 1)
                        sp.dma_start(w_raw[n][:, :], weight(s.layer + 1, "qkv"[n])).then_inc(w_loaded[n], 16)
                if s.u == UNITS + 1:
                    sp.wait_ge(outed, UNITS)
                    sp.dma_start(wo[:, 0, :, :], weight(2, "o").rearrange("(p r) e -> r p e", r=128)).then_inc(wo_loaded, 16)
                store(s)

            stream(sp, step)
            store(Step(N + 1))
            for v in range(2):
                sp.wait_ge(stored[v], 16 + 16 * UNITS // 2)

        @block.tensor
        def _(pe):
            mm = nc.tensor.matmul

            def split_product(dst, w, w_cols, x, x_cols, first=True, last=True):
                hi, lo = w
                xh, xl = x
                mm(dst, hi[w_cols], xh[x_cols], start=first, stop=False)
                mm(dst, hi[w_cols], xl[x_cols], start=False, stop=False)
                return mm(dst, lo[w_cols], xh[x_cols], start=False, stop=last)

            def scores(s, j):
                par, v = s.u // 2 % 2, s.u % 2
                if v == 0 and j == 0:
                    s.wait(pe, act_emptied, EMPTY_A.before)
                    s.wait(pe, dve_emptied, EMPTY_D.before)
                    if s.layer == 2:
                        s.wait(pe, rotated, ROTATED.before)
                        s.wait(pe, last_rotated, LAST_ROTATED.before)
                m = mask[:, 0 if s.layer == 0 else 1, bass.ds(local(s, 0), 1), :]
                mm(ps_s[j][:, :], eye_bf[:, :], m.broadcast_to([128, 8, S]), start=True, stop=False,
                   skip_group_check=True)
                for pp in range(HALF):
                    p = HALF * j + pp
                    for b in range(2):
                        t = (2 * v + b) * S
                        last = mm(ps_s[j][64 * b:64 * b + 64, 128 * pp:128 * pp + 128],
                                  qT[:, par, p, t:t + S], kT[:, par, p, 2 * v + b, :],
                                  start=False, stop=True, skip_group_check=True)
                last.then_inc(scored, 1)

            def weight_values(s, j):
                v = (s.u - 1) % 2
                if j == 0:
                    if s.u == N:
                        s.wait(pe, act_emptied, EMPTY_A.before)
                        s.wait(pe, dve_emptied, EMPTY_D.before)
                    s.wait(pe, out_read, lambda w: FIN1.at(w, 0) - 1)
                s.wait(pe, turn_read, lambda w: TURN.at(w - 1, "p", j))
                for pp in range(HALF):
                    for b in range(2):
                        last = mm(ps_o[j][64 * b:64 * b + 64, 128 * pp:128 * pp + 128],
                                  probsT[:, j, 128 * pp + 64 * b:128 * pp + 64 * b + 64],
                                  vv[:, v, b, HALF * j + pp, :], start=True, stop=True, skip_group_check=True)
                last.then_inc(weighted, 1)

            def turn(s, kind, j):
                if kind == "p":
                    s.wait(pe, exped, lambda w: TWICE.at(w, j))
                else:
                    s.wait(pe, weighted_read, lambda w: FIN2.at(w, j))
                if kind == "p" and finishes(s.u):
                    s.wait(pe, turn_read, lambda w: TURN.at(w, kind, j) - 2)
                src = probs if kind == "p" else heads
                for pp in range(HALF):
                    h = 2 * (HALF * j + pp)
                    last = nc.tensor.transpose(ps_t[j][:, 128 * pp:128 * pp + 128],
                                               src[:, h:h + 2, :].rearrange("q h k -> q (h k)"), eye[:, :])
                last.then_inc(turned, 1)

            def project_out(s):
                layer = (s.u - 1) // UNITS
                if s.times == 1:
                    pe.wait_ge(wo_loaded, 32 if layer < 2 else 48)
                for j in range(2):
                    if not attends(s.u):
                        s.wait(pe, turn_read, lambda w: TURN.at(w, "o", j))
                    for pp in range(HALF):
                        p = HALF * j + pp
                        last = mm(ps_o[0][:, 0:E], headsT[:, j, 128 * pp:128 * pp + 128], wo[:, layer % 2, p, :],
                                  start=(p == 0), stop=(p == PAIRS - 1))
                last.then_inc(outed, 1)

            def fill(s, at, name, j):
                u = s.u
                n = FILL.before(u) + at
                bank = ps_p[n % 2]
                if at == 0 and not (attends(u) and u % 2 == 0):
                    s.wait(pe, act_emptied, EMPTY_A.before)
                    s.wait(pe, dve_emptied, EMPTY_D.before)
                elif at >= 2:
                    before = fills(u)[:at - 1]
                    if "A" in before[-1][2]:
                        s.wait(pe, act_emptied, lambda w: EMPTY_A.before(w) + sum("A" in f[2] for f in before))
                    if "D" in before[-1][2]:
                        s.wait(pe, dve_emptied, lambda w: EMPTY_D.before(w) + sum("D" in f[2] for f in before))
                if name == "T":
                    s.wait(pe, chunk_loaded, lambda w: 32 * (projected(w) + 1))
                    for k in range(2 * CU):
                        last = nc.tensor.transpose(bank[:, 128 * k:128 * k + 128], chunk_in[:, k, :], eye[:, :])
                elif name == "V":
                    par, v = u // 2 % 2, u % 2
                    if j == 0 and s.times == 1:
                        pe.wait_ge(w_ready[2], s.layer + 1)
                    tok = slice(CT + 128 * v, CT + 128 * v + 128)
                    cols = (slice(None), slice(512 * j, 512 * j + 512))
                    x = (slice(None), par, tok)
                    mm(bank[:, :], inT_hi[x], w_hi[2][cols], start=True, stop=False)
                    mm(bank[:, :], inT_hi[x], w_lo[2][cols], start=False, stop=False)
                    last = mm(bank[:, :], inT_lo[x], w_hi[2][cols], start=False, stop=True)
                elif name[0] in "QK":
                    n_w = "QK".index(name[0])
                    g = projected(u)
                    x = (slice(None), g % 2, slice(CT * n_w, CT * n_w + CT))
                    if j == 0:
                        if not attends(u) or u % UNITS == 0:
                            pe.wait_ge(act_emptied, EMPTY_A.at(u - u % 2, "T", 0))
                            pe.wait_ge(dve_emptied, EMPTY_D.at(u - u % 2, "T", 0))
                        if s.times == 1:
                            pe.wait_ge(w_ready[n_w], g * 2 // UNITS + 1)
                    if (name[1:], j) == ("b", 0) and s.times == 1:
                        pe.wait_ge(swapped_ready[n_w], 1)
                    w = (sw_hi[n_w], sw_lo[n_w]) if name[1:] == "b" else (w_hi[n_w], w_lo[n_w])
                    for k in range(2):
                        p = 2 * j + k
                        last = split_product(bank[:, CT * k:CT * k + CT], w, (slice(None), slice(128 * p, 128 * p + 128)),
                                             (inT_hi, inT_lo), x, first=True)
                elif name == "FT":
                    s.wait(pe, pool_step, lambda w: PSTEP.at(w - 1, "out", 0))
                    for v in range(2):
                        k = (u - 3 + v) % 4
                        last = nc.tensor.transpose(bank[:, 128 * v:128 * v + 128], x2[:, k, :], eye[:, :])
                elif name == "F1":
                    for k in range(2):
                        c = 2 * j + k
                        last = split_product(bank[:, CT * k:CT * k + CT], (w1_hi, w1_lo),
                                             (slice(None), slice(128 * c, 128 * c + 128)),
                                             (x2T_hi, x2T_lo), (slice(None), slice(None)))
                else:
                    for v in range(2):
                        for c in range(FC):
                            last = mm(bank[:, E * v:E * v + E], hT[:, c, 128 * v:128 * v + 128], w2[:, c, :],
                                      start=(c == 0), stop=(c == FC - 1))
                last.then_inc(filled, 1)

            def step(s):
                for name, j, *at in plan(s.u):
                    if name == "S":
                        scores(s, j)
                    elif name == "AV":
                        weight_values(s, j)
                    elif name in ("OT", "PT"):
                        turn(s, name[0].lower(), j)
                    elif name == "Y":
                        project_out(s)
                    else:
                        fill(s, at[0], name, j)

            def before_0():
                pe.wait_ge(setup_pool, MASKED)

            def before_1():
                pe.wait_ge(wo_loaded, 32)
                pe.wait_ge(setup_dve, STAGED)
                for layer in range(2):
                    stage = [rope_a, rope_b][layer][:, :, :].rearrange("r h d -> r (h d)")
                    for p in range(PAIRS):
                        last = mm(ps_o[layer][:, 0:E], stage[:, 128 * p:128 * p + 128], wo[:, layer, p, :],
                                  start=(p == 0), stop=(p == PAIRS - 1))
                    last.then_inc(bvwo_done, 1)
                pe.wait_ge(bvwo_read, 2)
                pe.wait_ge(late_loaded, 32)
                pe.wait_ge(setup_pool, W1_SPLIT)

            pe.wait_ge(setup_pool, EYES)
            stream(pe, step, {0: before_0, 1: before_1})

        @block.scalar
        def _(act):
            def empty(s, at, name, j):
                u = s.u
                bank = ps_p[(FILL.before(u) + at) % 2]
                s.wait(act, filled, lambda w: FILL.before(w) + at + 1)
                if name == "T":
                    ins = nc.scalar.activation(inT_hi[:, projected(u) % 2, :], bank[:, :], ACT.Copy)
                elif name == "FT":
                    ins = nc.scalar.activation(x2T_hi[:, :], bank[:, 0:CT], ACT.Copy)
                elif name == "V":
                    pair = slice(HALF * j, HALF * j + HALF)
                    for b in range(2):
                        src = bank[64 * b:64 * b + 64, :].rearrange("k (p h d) -> k p h d", p=HALF, h=2)
                        for h in range(2):
                            ins = nc.scalar.activation(vv[64 * h:64 * h + 64, u % 2, b, pair, 64 * h:64 * h + 64],
                                                       src[:, :, h, :], ACT.Copy)
                elif name == "Q":
                    g = projected(u)
                    for k in range(2):
                        p = 2 * j + k
                        ins = nc.scalar.activation(qT[:, g % 2, p, :], bank[:, CT * k:CT * k + CT], ACT.Identity,
                                                   bias=bq[:, g * 2 // UNITS, p:p + 1])
                elif name == "K":
                    g = projected(u)
                    for k in range(2):
                        p = 2 * j + k
                        src = bank[0:64, CT * k:CT * k + CT].rearrange("d (b t) -> d b t", t=S)
                        ins = nc.scalar.activation(kT[0:64, g % 2, p, :, 0:64], src, ACT.Identity,
                                                   bias=bk[0:64, g * 2 // UNITS, p:p + 1])
                elif name == "F1":
                    for c in range(2):
                        ins = nc.scalar.activation(hT[:, c, :], bank[:, CT * c:CT * c + CT], ACT.Relu,
                                                   bias=b1[:, c:c + 1])
                ins.then_inc(act_emptied, 1)

            def turn_out(s, kind, j):
                s.wait(act, turned, lambda w: TURN.at(w, kind, j))
                dst = probsT if kind == "p" else headsT
                nc.scalar.activation(dst[:, j, :], ps_t[j][:, :], ACT.Copy).then_inc(turn_read, 1)

            def exponentials(s, j):
                s.wait(act, shifted, lambda w: TWICE.at(w, j))
                p = probs[:, 8 * j:8 * j + 8, :]
                nc.scalar.activation(p, p, ACT.Exp, scale=float(D) ** -0.5).then_inc(exped, 1)

            def split_high(s, after_input=False):
                if new_weights(s, after_input) is None:
                    return
                layer, n = new_weights(s, after_input)
                act.wait_ge(w_loaded[n], 16 * (layer + 1))
                if layer:
                    act.wait_ge(filled, FILL.before(s.u if n == 2 else s.u - 1))
                ins = nc.scalar.activation(w_hi[n][:, :], w_raw[n][:, :], ACT.Copy)
                if layer == 2 and n < 2:
                    for k in range(2):
                        ins = nc.scalar.activation(halves(sw_hi[n])[:, :, k], halves(w_raw[n])[:, :, 1 - k], ACT.Copy)
                ins.then_inc(w_hi_ready[n], 1)

            def step(s):
                split_high(s)
                who = [w for _, _, w in fills(s.u)]
                order = plan(s.u)
                names = [e[:2] for e in order]
                for name, j, *at in order:
                    if at and "A" in who[at[0]]:
                        empty(s, at[0], name, j)
                        if name == "T":
                            split_high(s, after_input=True)
                            if s.u == -2:
                                act.wait_ge(first_loaded, 96)
                    if name in ("OT", "PT"):
                        turn_out(s, name[0].lower(), j)
                    if attends(s.u) and ("AV", 0) in names and name == "AV":
                        exponentials(s, j)
                    if attends(s.u) and ("AV", 0) not in names and name == "Q" and j >= 2:
                        exponentials(s, j - 2)

            def before_m1():
                act.wait_ge(setup_pool, ZERO_K0)

            def before_0():
                act.wait_ge(setup_pool, ZEROED)
                act.wait_ge(const_loaded, 16 * N_CONST)

            stream(act, step, {-1: before_m1, 0: before_0})

        @block.vector
        def _(dve):
            V = nc.vector

            turn_v = [0]

            def carrier():
                turn_v[0] = turn_v[0] % 30 + 1
                V.tensor_copy(carried[:, turn_v[0]:turn_v[0] + 1], carried[:, 0:1])

            def empty(s, at, name, j):
                u = s.u
                bank = ps_p[(FILL.before(u) + at) % 2]
                if name[1:] == "a":
                    back = j - 1 if name == "Ka" else max(j - 1, 0)
                    s.wait(dve, rotated, lambda w: ROTATED.before(w) + back)
                if name not in ("T", "FT"):
                    s.wait(dve, filled, lambda w: FILL.before(w) + at + 1)
                if name in ("T", "FT"):
                    s.wait(dve, act_emptied, lambda w: EMPTY_A.at(w, name, j))
                    if name == "T":
                        par = projected(u) % 2
                        ins = V.tensor_tensor(inT_lo[:, par, :], bank[:, :], inT_hi[:, par, :].bitcast(F32), ALU.subtract)
                    else:
                        ins = V.tensor_tensor(x2T_lo[:, :], bank[:, 0:CT], x2T_hi[:, :].bitcast(F32), ALU.subtract)
                elif name == "Q":
                    g = projected(u)
                    for k in range(2):
                        p = 2 * j + k
                        ins = V.tensor_scalar(qT[:, g % 2, p, :], bank[:, CT * k:CT * k + CT],
                                              bq[:, g * 2 // UNITS, p:p + 1], None, ALU.add)
                elif name == "K":
                    g = projected(u)
                    for k in range(2):
                        p = 2 * j + k
                        src = bank[64:128, CT * k:CT * k + CT].rearrange("d (b t) -> d b t", t=S)
                        ins = V.tensor_scalar(kT[64:128, g % 2, p, :, 64:128], src,
                                              bk[64:128, g * 2 // UNITS, p:p + 1], None, ALU.add)
                elif name[1:] in ("a", "b"):
                    to, table = (rope_a, cos) if name[1:] == "a" else (rope_b, sin)
                    ins = V.tensor_tensor(to[:, j % 2, :].rearrange("d (b t) -> d b t", t=S),
                                          bank[:, :].rearrange("d (b t) -> d b t", t=S),
                                          table[:, None, :].broadcast_to([128, 8, S]), ALU.mult)
                elif name == "F1":
                    for k in range(2):
                        c = 2 + k
                        ins = V.tensor_scalar(hT[:, c, :], bank[:, CT * k:CT * k + CT], b1[:, c:c + 1], 0.0,
                                              ALU.add, ALU.max)
                elif name == "F2":
                    s.wait(dve, pool_step, lambda w: PSTEP.at(w, "fres"))
                    ins = V.tensor_tensor(fz[:, :, :], bank[:, 0:2 * E].rearrange("t (v e) -> t v e", v=2),
                                          fres[:, :, :], ALU.add)
                ins.then_inc(dve_emptied, 1)
                if (name, j) == ("Kb", 3):
                    s.wait(dve, dve_emptied, lambda w: EMPTY_D.at(w, "Kb", 3))
                    for h in range(2):
                        ins = add_keys(V, s, j, h)
                    ins.then_inc(last_rotated, 1)

            def maximum(s, j):
                s.wait(dve, scored, lambda w: TWICE.at(w, j))
                sc = ps_s[j][:, :].rearrange("q (h k) -> q h k", k=S)
                hs = slice(8 * j, 8 * j + 8)
                V.tensor_reduce(top[:, hs], sc, AX_X, ALU.max).then_inc(dve_step, 1)

            def shift(s, j):
                sc = ps_s[j][:, :].rearrange("q (h k) -> q h k", k=S)
                hs = slice(8 * j, 8 * j + 8)
                s.wait(dve, dve_step, lambda w: VSTEP.at(w, "max", j))
                V.tensor_tensor(probs[:, hs, :], sc, top[:, hs, None].broadcast_to([128, 8, S]), ALU.subtract)\
                 .then_inc(shifted, 1)

            def sums(s):
                s.wait(dve, exped, lambda w: TWICE.at(w, 1))
                V.tensor_reduce(total[:, :], probs[:, :, :], AX_X, ALU.add).then_inc(dve_step, 1)
                s.wait(dve, dve_step, lambda w: VSTEP.at(w, "sum"))
                V.reciprocal(inv[:, :], total[:, :]).then_inc(dve_step, 1)

            def inverse(s):
                s.wait(dve, dve_step, lambda w: VSTEP.at(w, "recip"))
                V.tensor_scalar(rinv[:, :], inv[:, :], valid[:, s.layer, bass.ds(local(s, 0), 1)], None, ALU.mult)\
                 .then_inc(dve_step, 1)

            def normalise(s, j):
                if j == 0 and not finishes(s.u - 1):
                    s.wait(dve, dve_step, VSTEP.before)
                s.wait(dve, weighted, lambda w: FIN2.at(w, j))
                hs = slice(8 * j, 8 * j + 8)
                V.tensor_tensor(heads[:, hs, :], ps_o[j][:, :].rearrange("q (h d) -> q h d", d=D),
                                rinv[:, hs, None].broadcast_to([128, 8, D]), ALU.mult).then_inc(weighted_read, 1)

            def tail(s):
                v = (s.u - 1) % 2
                s.wait(dve, outed, lambda w: FIN1.at(w, 0))
                s.wait(dve, pool_step, lambda w: PSTEP.at(w, "res"))
                V.tensor_tensor(z[:, v, :], ps_o[0][:, 0:E], res[:, :], ALU.add).then_inc(out_read, 1)
                s.wait(dve, out_read, lambda w: FIN1.at(w, 0))
                V.bn_stats(stat[:, :], z[:, v, :]).then_inc(dve_step, 1)
                s.wait(dve, dve_step, lambda w: VSTEP.at(w, "stat"), carrier)
                V.bn_aggr(mv[:, v, :], stat[:, :]).then_inc(dve_step, 1)

            def ffn_tail(s):
                s.wait(dve, dve_emptied, lambda w: EMPTY_D.at(w, "F2", 0))
                for v in range(2):
                    V.bn_stats(fstat[:, v, :], fz[:, v, :]).then_inc(dve_step, 1)
                for v in range(2):
                    s.wait(dve, dve_step, lambda w: VSTEP.at(w, "fstat", v), carrier)
                    V.bn_aggr(fmv[:, v, :], fstat[:, v, :]).then_inc(dve_step, 1)

            def split_rest(s, after_input=False):
                if new_weights(s, after_input) is None:
                    return
                layer, n = new_weights(s, after_input)
                dve.wait_ge(w_hi_ready[n], layer + 1)
                V.tensor_tensor(w_lo[n][:, :], w_raw[n][:, :], w_hi[n][:, :].bitcast(F32), ALU.subtract)\
                 .then_inc(w_ready[n], 1)

            def split_swapped(s):
                layer, n = new_weights(s) or (0, 0)
                if layer == 2 and n < 2:
                    for k in range(2):
                        ins = V.tensor_tensor(halves(sw_lo[n])[:, :, k], halves(w_raw[n])[:, :, 1 - k],
                                              halves(sw_hi[n]).bitcast(F32)[:, :, k], ALU.subtract)
                    ins.then_inc(swapped_ready[n], 1)

            def step(s):
                if not attends(s.u):
                    split_rest(s)
                who = [w for _, _, w in fills(s.u)]
                shift_next = None
                for name, j, *at in plan(s.u):
                    if shift_next is not None and not at:
                        shift(s, shift_next)
                        shift_next = None
                    if name == "S":
                        maximum(s, j)
                        shift_next = j
                        if new_weights(s) is not None and j == (new_weights(s)[1] == 2):
                            split_rest(s)
                        if j == 1:
                            split_swapped(s)
                    elif name == "AV":
                        normalise(s, j)
                    elif name == "Y":
                        if attends(s.u):
                            inverse(s)
                        tail(s)
                    elif at and "D" in who[at[0]]:
                        empty(s, at[0], name, j)
                        if name == "T":
                            split_rest(s, after_input=True)
                            if s.u == -2:
                                dve.wait_ge(first_loaded, 96)
                        if shift_next is not None:
                            shift(s, shift_next)
                            shift_next = None
                    if (name, j) == ("PT", 0 if ffn_chunk(s.u) is not None else 1):
                        sums(s)
                        if not finishes(s.u):
                            inverse(s)
                    if name == "F2":
                        ffn_tail(s)

            def before_m1():
                dve.wait_ge(mask_loaded, 32)
                for n in (0, 1):
                    V.tensor_scalar(mask[:, n, :, :], mask_u8[:, :, :], -NEG, NEG, ALU.mult, ALU.add).then_inc(setup_dve, 1)
                for layer, stage in enumerate((rope_a, rope_b)):
                    V.tensor_copy(stage[:, :, :].rearrange("r a (p d) -> r (a p) d", p=HALF),
                                  bv[:, layer, :, None].broadcast_to([128, PAIRS, 128])).then_inc(setup_dve, 1)
                dve.wait_ge(setup_pool, ZERO_K0)

            def before_0():
                dve.wait_ge(setup_pool, MASKED)
                dve.wait_ge(const_loaded, 16 * N_CONST)
                for n in range(2):
                    V.tensor_reduce(valid[:, n, :], mask[:, n, :, :], AX_X, ALU.max).then_inc(setup_dve, 1)
                dve.wait_ge(setup_dve, VALID - 1)
                V.tensor_scalar(valid[:, 0:2, :], valid[:, 0:2, :], NEG / 2, None, ALU.is_gt).then_inc(setup_dve, 1)
                dve.wait_ge(setup_dve, VALID)

            def before_1():
                for layer in range(2):
                    dve.wait_ge(bvwo_done, layer + 1)
                    V.tensor_copy(bvwo[:, layer, :], ps_o[layer][:, 0:E]).then_inc(bvwo_read, 1)

            V.memset(carried[:, 0:1], 0.0)
            V.memset(valid[:, 2, :], 1.0)
            stream(dve, step, {-1: before_m1, 0: before_0, 1: before_1})

        @block.gpsimd
        def _(pool):
            G = nc.gpsimd

            turn_g = [0]

            def carrier():
                turn_g[0] = turn_g[0] % 31 + 1
                n, zero = 32 + turn_g[0], carried[:, 32:33]
                G.tensor_tensor(carried[:, n:n + 1], zero, zero, ALU.add)

            def chain(s, *event, to=None):
                s.wait(pool, pool_step, lambda w: PSTEP.at(w, *event), to)

            def settled(s, *event, to=None):
                s.wait(pool, pool_step, lambda w: PSTEP.at(w, *event) - 1, to)

            def rotate(s):
                for j in range(3 if s.u % 2 else 4):
                    name = "K" if s.u % 2 else "Q"
                    par = projected(s.u) % 2
                    s.wait(pool, dve_emptied, lambda w: EMPTY_D.at(w, name + "b", j))
                    if name == "Q":
                        G.tensor_tensor(qT[:, par, 2 * j:2 * j + 2, :].rearrange("d p t -> d (p t)"),
                                        rope_a[:, j % 2, :], rope_b[:, j % 2, :], ALU.add).then_inc(rotated, 1)
                    else:
                        for h in range(2):
                            if h:
                                s.wait(pool, rope_part, lambda w: PARTS.at(w, j))
                            elif j:
                                s.wait(pool, rotated, lambda w: ROTATED.at(w, "Kb", j - 1))
                            add_keys(G, s, j, h).then_inc(rotated if h else rope_part, 1)
                if s.u % 2:
                    s.wait(pool, rotated, lambda w: ROTATED.at(w, "Kb", 2))

            def residual(s):
                if not finishes(s.u):
                    return
                layer = (s.u - 1) // UNITS
                unit = bass.ds(local(s, -1), 1)
                s.wait(pool, out_read, lambda w: FIN1.at(w, 0) - 1, carrier if layer == 2 else None)
                if layer < 2:
                    settled(s, "rbias")
                    G.tensor_tensor(zn[:, :], bvwo[:, layer, :], valid[:, layer, unit].broadcast_to([128, E]), ALU.mult)\
                     .then_inc(pool_step, 1)
                    chain(s, "rbias")
                    G.tensor_tensor(zn[:, :], zn[:, :], bo[:, layer, :], ALU.add).then_inc(pool_step, 1)
                    chain(s, "rbo", to=carrier)
                    G.tensor_tensor(res[:, None, :], zn[:, None, :], X[:, unit, :], ALU.add).then_inc(pool_step, 1)
                else:
                    settled(s, "rbias", to=carrier)
                    G.tensor_copy(res[:, None, 0:32], X[:, unit, 0:32]).then_inc(pool_step, 1)
                    G.tensor_copy(res[:, None, 32:64], X[:, unit, 32:64]).then_inc(pool_step, 1)
                    G.tensor_copy(res[:, None, 64:128], X[:, unit, 64:128]).then_inc(pool_step, 1)

            def layer_norm(s, pre, v, src, stats, dst, n, eps):
                tt = G.tensor_tensor
                settled(s, pre + "eps", v)
                tt(small[:, 0:1], stats[:, 1:2], epsilon[:, eps:eps + 1], ALU.add).then_inc(pool_step, 1)
                chain(s, pre + "eps", v)
                tt(small[:, 1:2], small[:, 0:1], minus_half[:, :], ALU.pow).then_inc(pool_step, 1)
                chain(s, pre + "rstd", v)
                tt(small[:, 2:3], stats[:, 0:1], small[:, 1:2], ALU.mult).then_inc(pool_step, 1)
                tt(zn[:, :], src, small[:, 1:2].broadcast_to([128, E]), ALU.mult).then_inc(pool_step, 1)
                chain(s, pre + "scaled", v)
                tt(zn[:, :], zn[:, :], small[:, 2:3].broadcast_to([128, E]), ALU.subtract).then_inc(pool_step, 1)
                chain(s, pre + "norm", v)
                tt(zn[:, :], zn[:, :], gain[:, n, :], ALU.mult).then_inc(pool_step, 1)
                chain(s, pre + "gain", v, to=carrier)
                tt(dst, zn[:, None, :], shift[:, n:n + 1, :], ALU.add).then_inc(pool_step, 1)

            def step(s):
                residual(s)
                if projected(s.u) is not None and projected(s.u) * 2 // UNITS == 2:
                    rotate(s)
                if ffn_chunk(s.u) is not None:
                    k = (s.u - 3) % 4
                    chain2 = PSTEP.at(s.u - 1, "out", 0)
                    s.wait(pool, pool_step, lambda w: PSTEP.at(w - 1, "out", 0))
                    G.tensor_tensor(fres[:, :, :], x2[:, k:k + 2, :], b2[:, None, :].broadcast_to([128, 2, E]),
                                    ALU.add).then_inc(pool_step, 1)
                    for v in range(2):
                        s.wait(pool, dve_step, lambda w: VSTEP.at(w, "fmv", v))
                        layer_norm(s, "f", v, fz[:, v, :], fmv[:, v, :], X[:, bass.ds(local(s, -3 + v), 1), :], 2, 0)
                if finishes(s.u):
                    layer, v = (s.u - 1) // UNITS, (s.u - 1) % 2
                    s.wait(pool, dve_step, lambda w: VSTEP.at(w, "mv"))
                    if layer == 2:
                        s.wait(pool, stored[v], lambda w: (w - 1 - 2 * UNITS) // 2 * 16 + 16)
                    dst = [X[:, bass.ds(local(s, -1), 1), :], x2[:, (s.u - 1) % 4:(s.u - 1) % 4 + 1, :],
                           y_out[:, v:v + 1, :]][layer]
                    layer_norm(s, "", 0, z[:, v, :], mv[:, v, :], dst, [0, 1, 3][layer], [0, 0, 1][layer])

            G.memset(eye[:, :], 0.0).then_inc(setup_pool, 1)
            G.memset(eye_bf[:, :], 0.0).then_inc(setup_pool, 1)
            pool.wait_ge(setup_pool, 2)
            for t in (eye, eye_bf):
                G.affine_select(out=t[:, :], in_=t[:, :], compare_op=ALU.not_equal, fill=1.0, base=0,
                                pattern=[[-1, 128]], channel_multiplier=1).then_inc(setup_pool, 1)
            G.memset(kT[:, 0, :, :, :], 0.0).then_inc(setup_pool, 1)
            G.memset(vv[:, :, :, :, :], 0.0).then_inc(setup_pool, 1)
            G.memset(kT[:, 1, :, :, :], 0.0).then_inc(setup_pool, 1)
            for v in range(2):
                G.memset(y_out[:, v, :], 0.0).then_inc(stored[v], 16)
            G.memset(minus_half[:, :], -0.5)
            G.memset(epsilon[:, 0:1], 1e-12)
            G.memset(epsilon[:, 1:2], 1e-3).then_inc(setup_pool, 1)
            G.memset(carried[:, 32:33], 0.0).then_inc(setup_pool, 1)
            pool.wait_ge(setup_dve, PADDED)
            for b in range(2):
                m = mask[64 * b:64 * b + 64, 0, :, :]
                if b:
                    pool.wait_ge(setup_pool, MASKED - 1)
                G.affine_select(out=m, in_=m, compare_op=ALU.is_ge, fill=NEG, base=0,
                                pattern=[[0, UNITS], [-1, S]], channel_multiplier=1).then_inc(setup_pool, 1)
            pool.wait_ge(setup_pool, MASKED)
            pool.wait_ge(w1_loaded, 16)
            G.tensor_copy(w1_hi[:, :], w1_raw).then_inc(setup_pool, 1)
            pool.wait_ge(setup_pool, MASKED + 1)
            G.tensor_tensor(w1_lo[:, :], w1_raw, w1_hi[:, :].bitcast(F32), ALU.subtract).then_inc(setup_pool, 1)
            pool.wait_ge(const_loaded, 16 * N_CONST)
            pool.wait_ge(x_loaded, 16)
            pool.wait_ge(bvwo_read, 2)
            stream(pool, step)


_INS = ['x', 'ctx_1024', 'mask_BxS2_bf1',
        'L0_xattn_sa_wq', 'L0_xattn_sa_bq', 'L0_xattn_sa_wk', 'L0_xattn_sa_bk', 'L0_xattn_sa_wv', 'L0_xattn_sa_bv',
        'L0_xattn_sa_wo', 'L0_xattn_sa_bo', 'L0_xattn_ca_wq', 'L0_xattn_ca_bq', 'L0_xattn_ca_wk', 'L0_xattn_ca_bk',
        'L0_xattn_ca_wv', 'L0_xattn_ca_bv', 'L0_xattn_ca_wo', 'L0_xattn_ca_bo', 'L0_xattn_ffn_w1', 'L0_xattn_ffn_b1',
        'L0_xattn_ffn_w2', 'L0_xattn_ffn_b2', 'L0_xattn_ln1_g', 'L0_xattn_ln1_b', 'L0_xattn_ln2_g', 'L0_xattn_ln2_b',
        'L0_xattn_ln3_g', 'L0_xattn_ln3_b', 'L1_xattn_Wq', 'L1_xattn_Wk', 'L1_xattn_Wv', 'L1_xattn_Wo',
        'L1_xattn_ln_gamma', 'L1_xattn_ln_beta']


def rotary_tables():
    inv_freq = (1.0 / 10000.0 ** (np.arange(0, D, 2, dtype=np.float32) / np.float32(D))).astype(np.float32)
    angle = np.arange(S, dtype=np.float32)[None, :] * np.tile(np.repeat(inv_freq, 2), 2)[:, None]
    sign = np.tile(np.array([-1.0, 1.0], np.float32), D)[:, None]
    return np.cos(angle).astype(np.float32), (np.sin(angle) * sign).astype(np.float32)


def kernel(**inputs):
    import concourse.bacc as bacc
    from concourse.bass_utils import run_bass_kernel_spmd

    nc = bacc.Bacc("TRN2", target_bir_lowering=False, num_devices=1)
    arrays = {name: np.ascontiguousarray(inputs[name]) for name in _INS}
    arrays["mask_BxS2_bf1"] = arrays["mask_BxS2_bf1"].view(np.uint8)
    for name in ["L0_xattn_" + n for n in ("sa_bq", "sa_bk", "sa_bv", "ca_bq", "ca_bk", "ca_bv", "ffn_b1")]:
        arrays[name] = np.ascontiguousarray(arrays[name].reshape(-1, 128).T)
    arrays["rope_cos"], arrays["rope_sin"] = rotary_tables()
    aps = {name: nc.dram_tensor("in_" + name, v.shape, mybir.dt.from_np(v.dtype), kind="ExternalInput").ap()
           for name, v in arrays.items()}
    out = nc.dram_tensor("out_0", (B, S, E), F32, kind="ExternalOutput").ap()
    build(nc, aps, out)
    r = run_bass_kernel_spmd(nc, [{"in_" + name: v for name, v in arrays.items()}], core_ids=[0])
    return r.results[0]["out_0"]
```
